# Optimizing a Trainium2 kernel written in Bass

```python
import numpy as np
import jax
import jax.numpy as jnp

def _softmax(x, axis=-1):
    return jax.nn.softmax(x, axis=axis)

def _gelu(x):
    return jax.nn.gelu(x, approximate=True)

def _silu(x):
    return jax.nn.silu(x)

def _sigmoid(x):
    return jax.nn.sigmoid(x)

def _layernorm(x, axis=-1, eps=1e-05):
    m = jnp.mean(x, axis=axis, keepdims=True)
    v = jnp.var(x, axis=axis, keepdims=True)
    return (x - m) / jnp.sqrt(v + eps)

def _scatter_add(tgt, idx, src, axis=0):
    return tgt.at[idx].add(src)

def _segment_sum(src, seg, n):
    return jax.ops.segment_sum(src, seg, n)
kernel_name = 'mk_prb_d1_jaxref_r4_befe05'

def setup_inputs(seed: int=0):
    np.random.seed(seed)
    _w = jnp.asarray

    def _L0_attn_setup():
        import jax, jax.numpy as jnp
        import numpy as np
        import math
        B, S, E, H = (2, 512, 256, 16)
        HD = E // H
        HX = 64
        P = HX // 2

        def _l2norm(x, eps=1e-12):
            n = jnp.sqrt(jnp.sum(x * x, axis=-1, keepdims=True))
            return x / jnp.maximum(n, eps)

        def _scramble(t):
            b, h, p, s, _ = t.shape
            return jnp.swapaxes(t, -1, -2).reshape(b, h, p, s, 2)
        key = jax.random.key(seed)
        ks = jax.random.split(key, 12)
        sc = 0.02
        return {'x': jax.random.normal(ks[0], (B, S, E), dtype=jnp.float32), 'Wq': jax.random.normal(ks[1], (E, E), dtype=jnp.float32) * sc, 'bq': jnp.zeros((E,), dtype=jnp.float32), 'Wk': jax.random.normal(ks[2], (E, E), dtype=jnp.float32) * sc, 'bk': jnp.zeros((E,), dtype=jnp.float32), 'Wv': jax.random.normal(ks[3], (E, E), dtype=jnp.float32) * sc, 'bv': jnp.zeros((E,), dtype=jnp.float32), 'Wo': jax.random.normal(ks[4], (E, E), dtype=jnp.float32) * sc, 'bo': jnp.zeros((E,), dtype=jnp.float32), 'Whel': jax.random.normal(ks[5], (H, HX, HD), dtype=jnp.float32) * sc, 'bhel': jnp.zeros((H, HX), dtype=jnp.float32)}
    _L0_attn_in = _L0_attn_setup()

    def _L0_ffn_setup():
        import jax, jax.numpy as jnp
        import numpy as np
        E = 8
        K = 2
        key = jax.random.key(seed)
        ks = jax.random.split(key, 8)
        B, T, d = (4, 512, 256)
        h = 4 * d // E
        s = 0.02
        X = jax.random.normal(ks[0], (B, T, d), jnp.float32)
        routing_W = jax.random.normal(ks[1], (E, d), jnp.float32) * s
        expert_bias = jnp.zeros((E,), jnp.float32)
        sW1 = jax.random.normal(ks[2], (d, h), jnp.float32) * s
        sb1 = jnp.zeros((h,), jnp.float32)
        sW2 = jax.random.normal(ks[3], (h, d), jnp.float32) * s
        sb2 = jnp.zeros((d,), jnp.float32)
        rW1 = jax.random.normal(ks[4], (E, d, h), jnp.float32) * s
        rb1 = jnp.zeros((E, h), jnp.float32)
        rW2 = jax.random.normal(ks[5], (E, h, d), jnp.float32) * s
        rb2 = jnp.zeros((E, d), jnp.float32)
        return dict(X=X, routing_W=routing_W, expert_bias=expert_bias, sW1=sW1, sb1=sb1, sW2=sW2, sb2=sb2, rW1=rW1, rb1=rb1, rW2=rW2, rb2=rb2)
    _L0_ffn_in = _L0_ffn_setup()
    _d = {'L0_attn_x': _L0_attn_in['x'], 'L0_attn_Wq': _L0_attn_in['Wq'], 'L0_attn_bq': _L0_attn_in['bq'], 'L0_attn_Wk': _L0_attn_in['Wk'], 'L0_attn_bk': _L0_attn_in['bk'], 'L0_attn_Wv': _L0_attn_in['Wv'], 'L0_attn_bv': _L0_attn_in['bv'], 'L0_attn_Wo': _L0_attn_in['Wo'], 'L0_attn_bo': _L0_attn_in['bo'], 'L0_attn_Whel': _L0_attn_in['Whel'], 'L0_attn_bhel': _L0_attn_in['bhel'], 'L0_ffn_routing_W': _L0_ffn_in['routing_W'], 'L0_ffn_expert_bias': _L0_ffn_in['expert_bias'], 'L0_ffn_sW1': _L0_ffn_in['sW1'], 'L0_ffn_sb1': _L0_ffn_in['sb1'], 'L0_ffn_sW2': _L0_ffn_in['sW2'], 'L0_ffn_sb2': _L0_ffn_in['sb2'], 'L0_ffn_rW1': _L0_ffn_in['rW1'], 'L0_ffn_rb1': _L0_ffn_in['rb1'], 'L0_ffn_rW2': _L0_ffn_in['rW2'], 'L0_ffn_rb2': _L0_ffn_in['rb2']}
    _x0 = _d['L0_attn_x']
    _d['L0_attn_x'] = jax.random.normal(jax.random.fold_in(jax.random.key(seed), 1), (4, 2048, 256), dtype=_x0.dtype)
    del _x0
    return _d

def reference(L0_attn_x, L0_attn_Wq, L0_attn_bq, L0_attn_Wk, L0_attn_bk, L0_attn_Wv, L0_attn_bv, L0_attn_Wo, L0_attn_bo, L0_attn_Whel, L0_attn_bhel, L0_ffn_routing_W, L0_ffn_expert_bias, L0_ffn_sW1, L0_ffn_sb1, L0_ffn_sW2, L0_ffn_sb2, L0_ffn_rW1, L0_ffn_rb1, L0_ffn_rW2, L0_ffn_rb2):

    def _L0_attn_ref(x, Wq, bq, Wk, bk, Wv, bv, Wo, bo, Whel, bhel):
        import jax, jax.numpy as jnp
        import numpy as np
        import math
        B, S, E, H = (2, 512, 256, 16)
        HD = E // H
        HX = 64
        P = HX // 2

        def _l2norm(x, eps=1e-12):
            n = jnp.sqrt(jnp.sum(x * x, axis=-1, keepdims=True))
            return x / jnp.maximum(n, eps)

        def _scramble(t):
            b, h, p, s, _ = t.shape
            return jnp.swapaxes(t, -1, -2).reshape(b, h, p, s, 2)
        b, s, e = x.shape
        h, hx, hd = Whel.shape
        p = hx // 2
        q = x @ Wq.T + bq
        k = x @ Wk.T + bk
        v = x @ Wv.T + bv
        qh = q.reshape(b, s, h, hd)
        kh = k.reshape(b, s, h, hd)
        q_hel = jnp.einsum('bshd,hed->bshe', qh, Whel) + bhel
        k_hel = jnp.einsum('bshd,hed->bshe', kh, Whel) + bhel
        qn = _l2norm(q_hel.reshape(b, s, h, p, 2)).transpose(0, 2, 3, 1, 4)
        kn = _l2norm(k_hel.reshape(b, s, h, p, 2)).transpose(0, 2, 3, 1, 4)
        qn = _scramble(qn)
        kn = _scramble(kn)
        helical = jnp.einsum('bhpsc,bhptc->bhst', qn, kn) / p
        dot = jnp.einsum('bshd,bthd->bhst', qh, kh) / math.sqrt(hd)
        alpha = 0.5
        attn = jax.nn.softmax(alpha * dot + (1.0 - alpha) * helical, axis=-1)
        vh = v.reshape(b, s, h, hd)
        out = jnp.einsum('bhst,bthd->bshd', attn, vh).reshape(b, s, e)
        return out @ Wo.T + bo

    def _L0_ffn_ref(X, routing_W, expert_bias, sW1, sb1, sW2, sb2, rW1, rb1, rW2, rb2):
        import jax, jax.numpy as jnp
        import numpy as np
        E = 8
        K = 2
        B, T, d = X.shape
        shared = jax.nn.silu(X @ sW1 + sb1) @ sW2 + sb2
        logits = jnp.einsum('btd,ed->bte', X, routing_W) + expert_bias
        activation = jnp.sqrt(jax.nn.softplus(logits))
        top_vals, top_idx = jax.lax.top_k(activation, K)
        combine = jnp.sum(jax.nn.one_hot(top_idx, E, dtype=X.dtype) * top_vals[..., None], axis=-2)
        Xf = X.reshape(-1, d)
        cf = combine.reshape(-1, E)
        hdn = jax.nn.silu(jnp.einsum('nd,edh->enh', Xf, rW1) + rb1[:, None, :])
        y = jnp.einsum('enh,ehd->end', hdn, rW2) + rb2[:, None, :]
        routed = jnp.einsum('ne,end->nd', cf, y).reshape(B, T, d)
        return shared + routed
    x = L0_attn_x
    xn = _layernorm(x, axis=-1)
    x = x + _L0_attn_ref(xn, L0_attn_Wq, L0_attn_bq, L0_attn_Wk, L0_attn_bk, L0_attn_Wv, L0_attn_bv, L0_attn_Wo, L0_attn_bo, L0_attn_Whel, L0_attn_bhel) + _L0_ffn_ref(xn, L0_ffn_routing_W, L0_ffn_expert_bias, L0_ffn_sW1, L0_ffn_sb1, L0_ffn_sW2, L0_ffn_sb2, L0_ffn_rW1, L0_ffn_rb1, L0_ffn_rW2, L0_ffn_rb2)
    return x

_drawn_inputs = setup_inputs


def setup_inputs(seed=0):
    import zlib

    import numpy as np

    out = dict(_drawn_inputs(seed))
    spreads = {'L0_attn_bq': (0.0, 0.8),
     'L0_attn_bk': (0.0, 2.0),
     'L0_attn_bv': (0.0, 0.279),
     'L0_attn_bo': (0.0, 0.1),
     'L0_attn_bhel': (0.0, 2.0),
     'L0_ffn_expert_bias': (0.0, 0.1),
     'L0_ffn_sb1': (0.0, 0.736),
     'L0_ffn_sb2': (0.0, 0.1),
     'L0_ffn_rb1': (0.0, 0.502),
     'L0_ffn_rb2': (0.0, 0.1)}
    factors = {'L0_attn_Wq': 8.0, 'L0_attn_Wk': 8.0, 'L0_attn_Wv': 8.0, 'L0_attn_Whel': 43.742}
    for name, (base, spread) in spreads.items():
        noise = np.random.default_rng([zlib.crc32(name.encode()), seed]).standard_normal(out[name].shape)
        drawn = base * np.exp(spread * noise) if base else spread * noise
        out[name] = jnp.asarray(drawn.astype(out[name].dtype))
    for name, factor in factors.items():
        out[name] = (out[name] * factor).astype(out[name].dtype)
    return out
```

```python
from contextlib import ExitStack

import numpy as np

import concourse.bass as bass
from concourse import mybir

F32 = mybir.dt.float32
F32R = mybir.dt.float32r
ALU = mybir.AluOpType
ACT = mybir.ActivationFunctionType
AX = mybir.AxisListType

B, S, E, H = 4, 2048, 256, 16
D = E // H
HX = 64
NE, FH = 8, 128
NX = NE + 1
P = 128
N = B * S
NH = B * H
EC = E // P
TOK = 512
TILES = S // TOK
SUB = TOK // P
TB = S // P
HALF = S // 2
QK_COL, VR_COL, W1_COL = 0, 2 * E, 2 * E + E + NE
VR = E + NE
WCOLS = W1_COL + NX * FH
GROWS = 6 * D + 2
LN_EPS = 1e-5
NORM_EPS2 = 1e-24
LN_SET = "natural_log_exp_and_others"
LOG_SCALE = 2.0 ** 16
SAFE = 1e30
LOG_SHIFT = 8.0 * float(np.log(2.0))


def wait(eng, semaphore, value):
    if not isinstance(value, int) or value > 0:
        eng.wait_ge(semaphore, value)


def split_weights(nc, a):
    with ExitStack() as ctx:
        sem = lambda name: ctx.enter_context(nc.semaphore(name))
        sb = lambda name, shape, dt: ctx.enter_context(nc.sbuf_tensor("sb_" + name, shape, dt))
        raw = sb("w_raw", [P, EC, WCOLS], F32)
        hel_raw = sb("hel_raw", [GROWS, H * 2 * P], F32)
        hel_rounded = sb("hel_rounded", [GROWS, H * 2 * P], F32R)
        hel_split = sb("hel_split", [GROWS, H * 2 * P], F32R)
        low_row = sb("low_row", [GROWS, 1], F32)
        w_in, hel_in, small_in = sem("w_in"), sem("hel_in"), sem("small_in")
        hi_done, hel_rounded_done, hel_done, lo_done, hel_out = (
            sem("hi_done"), sem("hel_rounded_done"), sem("hel_done"), sem("lo_done"), sem("hel_out"))
        with nc.Block() as block:

            @block.sync
            def _(sp):
                sp.dma_start(hel_raw[:, :], a["hel_w"]).then_inc(hel_in, 16)
                sp.dma_start(low_row[:, :], a["low_row"]).then_inc(hel_in, 16)
                sp.dma_start(raw[:, :, :], a["wcat"].rearrange("(c p) n -> p c n", p=P)).then_inc(w_in, 16)
                sp.dma_start(a["ident_sb"][:, :], a["ident"]).then_inc(small_in, 16)
                sp.dma_start(a["w2_sb"][:, :, :], a["w2"]).then_inc(small_in, 16)
                sp.dma_start(a["b2_sb"][:, :], a["b2"]).then_inc(small_in, 16)
                sp.dma_start(a["bqk_sb"][:, :], a["bqk"]).then_inc(small_in, 16)
                sp.dma_start(a["b1_sb"][:, :], a["b1"]).then_inc(small_in, 16)
                sp.dma_start(a["bvr_sb"][:, :], a["bvr"].partition_broadcast(P)).then_inc(small_in, 16)
                sp.dma_start(a["earlier_sb"][:, :], a["earlier"].partition_broadcast(P)).then_inc(small_in, 16)
                sp.wait_ge(small_in, 7 * 16)
                sp.wait_ge(hel_done, 1)
                for b in range(B):
                    sp.dma_start(a["WS"][b * H:(b + 1) * H].rearrange("h k n -> k h n"),
                                 hel_split[:, :].bitcast(F32).rearrange("k (h n) -> k h n", h=H)).then_inc(hel_out, 16)
                sp.wait_ge(hel_out, B * 16)

            @block.vector
            def _(dve):
                dve.wait_ge(hel_in, 32)
                dve.tensor_copy(hel_rounded[:, :], hel_raw[:, :]).then_inc(hel_rounded_done, 1)
                dve.wait_ge(hel_rounded_done, 1)
                dve.scalar_tensor_tensor(out=hel_split[:, :], in0=hel_rounded[:, :].bitcast(F32), scalar=low_row[:, 0:1],
                                         in1=hel_raw[:, :], op0=ALU.mult, op1=ALU.add).then_inc(hel_done, 1)
                dve.wait_ge(w_in, 16)
                for c in range(EC):
                    last = dve.tensor_copy(a["w_hi"][:, c, :], raw[:, c, :])
                last.then_inc(hi_done, 1)
                dve.wait_ge(hi_done, 1)
                for c in range(EC):
                    last = dve.tensor_tensor(a["w_lo"][:, c, :], raw[:, c, :], a["w_hi"][:, c, :].bitcast(F32), ALU.subtract)
                last.then_inc(lo_done, 1)
                dve.wait_ge(lo_done, 1)


def tokens(nc, a):
    with ExitStack() as ctx:
        sem = lambda name: ctx.enter_context(nc.semaphore(name))
        sb = lambda name, shape, dt=F32: ctx.enter_context(nc.sbuf_tensor("sb_" + name, shape, dt))
        x = sb("x", [P, 4, SUB, E])
        stats = sb("stats", [P, SUB, 6])
        spare = sb("spare", [P, 1])
        eps = sb("eps", [P, SUB])
        mean_var = sb("mean_var", [P, 2, SUB, 2])
        rstd = sb("rstd", [P, 2, SUB])
        powers = sb("powers", [P, 2, SUB * NE])
        xn = sb("xn", [P, 2, SUB, E])
        xt_hi = sb("xt_hi", [P, 2, EC, TOK], F32R)
        xt_lo = sb("xt_lo", [P, 2, EC, TOK], F32R)
        qk_hi = sb("qk_hi", [P, 4, TOK], F32R)
        qk_lo = sb("qk_lo", [P, 4, TOK], F32R)
        v = sb("v", [P, H, TB, D])
        logit = sb("logit", [P, SUB, NE])
        absl = sb("absl", [P, SUB, NE])
        ex = sb("ex", [P, SUB, NE])
        one_ex = sb("one_ex", [P, SUB, NE])
        lost = sb("lost", [P, SUB, NE])
        inv = sb("inv", [P, SUB, NE])
        logs = sb("logs", [P, SUB, NE])
        soft = sb("soft", [P, SUB, NE])
        log_soft = sb("log_soft", [P, SUB, NE])
        softplus = sb("softplus", [P, SUB, NE])
        active = sb("active", [P, SUB, NE])
        above = sb("above", [P, SUB, NE, NE])
        level = sb("level", [P, SUB, NE, NE])
        rank = sb("rank", [P, SUB, NE])
        gate = sb("gate", [P, 2, SUB, NE + 2])
        gate_t = sb("gate_t", [P, TOK])
        hid = sb("hid", [P, NX, TOK])
        y = sb("y", [P, 2, SUB, E])

        ps = ctx.enter_context(nc.psum_tensor("ps_tokens", [P, 8, 512], F32))
        ps_t, ps_a, ps_v, ps_y = ps[:, 0:2, :], ps[:, 2:4, :], ps[:, 4:6, :], ps[:, 6:8, :]

        x_in = [sem(f"x_in{j}") for j in range(4)]
        mean_ready, rstd_ready, xn_ready, xt_ready, xt_hi_ready, xt_lo_ready = (
            sem("mean_ready"), sem("rstd_ready"), sem("xn_ready"), sem("xt_ready"), sem("xt_hi_ready"), sem("xt_lo_ready"))
        const_ready, vr_ready, vr_out, qk_ready, qk_hi_ready, qk_lo_ready = (
            sem("const_ready"), sem("vr_ready"), sem("vr_out"), sem("qk_ready"), sem("qk_hi_ready"), sem("qk_lo_ready"))
        hidden_ready, silu_done, unit_ready, unit_out, y_step = (
            sem("hidden_ready"), sem("silu_done"), sem("unit_ready"), sem("unit_out"), sem("y_step"))
        router_step, exp_ready, log_ready, soft_ready, active_ready, gate_ready, gate_t_ready, gate_t_out = (
            sem("router_step"), sem("exp_ready"), sem("log_ready"), sem("soft_ready"), sem("active_ready"),
            sem("gate_ready"), sem("gate_t_ready"), sem("gate_t_out"))
        ln_step, stats_ready, rank_ready = sem("ln_step"), sem("stats_ready"), sem("rank_ready")
        qk_out = [sem(f"qk_out{m}") for m in range(4)]
        v_out, y_out = [sem(f"v_out{j}") for j in range(TILES)], [sem(f"y_out{j}") for j in range(2)]

        ROUTER_STEPS = 9
        UNITS = 5

        with nc.Block() as block:

            @block.sync
            def _(sp):
                def load_x(t, j):
                    sp.dma_start(x[:, j], a["x"][bass.ds(t * TOK, TOK), :].rearrange("(s p) e -> p s e", p=P)).then_inc(x_in[j], 16)

                for j in range(2):
                    load_x(j, j)

                def batch(b, last):
                    for j in range(TILES):
                        t = b * TILES + j
                        if not (last and j >= 2):
                            load_x(t + 2, (j + 2) % 4)
                        for m in range(4):
                            dst = a["QS"] if m < 2 else a["KS"]
                            rows = dst[bass.ds(b * H + (m % 2) * 8, 8)]
                            for part, (src, ready) in enumerate(((qk_hi, qk_hi_ready), (qk_lo, qk_lo_ready))):
                                sp.wait_ge(ready, t * 4 + m + 1)
                                sp.dma_start(rows[:, part, :, j * TOK:(j + 1) * TOK],
                                             src[:, m, :].bitcast(F32)).then_inc(qk_out[m], 16)
                        sp.wait_ge(vr_out, (t + 1) * SUB)
                        sp.dma_start(a["VS"][bass.ds(b * H, H), :, j * SUB * D:(j + 1) * SUB * D].rearrange("h p k -> p h k"),
                                     v[:, :, j * SUB:(j + 1) * SUB, :].rearrange("p h k d -> p h (k d)")).then_inc(v_out[j], 16)
                        sp.wait_ge(unit_out, (t + 1) * SUB * UNITS)
                        sp.dma_start(a["PART"][bass.ds(t * TOK, TOK), :].rearrange("(s p) e -> p s e", p=P),
                                     y[:, j % 2]).then_inc(y_out[j % 2], 16)

                batch(0, False)
                with sp.Fori(1, B - 1) as b:
                    batch(b, False)
                batch(B - 1, True)
                for m in range(4):
                    sp.wait_ge(qk_out[m], B * TILES * 32)
                for j in range(TILES):
                    sp.wait_ge(v_out[j], B * 16)
                for j in range(2):
                    sp.wait_ge(y_out[j], B * TILES // 2 * 16)

            @block.gpsimd
            def _(pool):
                pool.memset(powers[:, 0, :], -0.5)
                pool.memset(powers[:, 1, :], 0.5)
                pool.memset(eps[:, :], LN_EPS)
                pool.memset(gate[:, :, :, :], 1.0)
                pool.memset(gate_t[:, :], 0.0).then_inc(const_ready, 1)
                pool.wait_ge(const_ready, 1)

                def rstd_of(t, j):
                    pool.wait_ge(mean_ready, t + 1)
                    pool.tensor_tensor(mean_var[:, j % 2, :, 1], mean_var[:, j % 2, :, 1], eps[:, :], ALU.add).then_inc(ln_step, 1)
                    pool.wait_ge(ln_step, t + 1)
                    pool.tensor_tensor(rstd[:, j % 2, :], mean_var[:, j % 2, :, 1], powers[:, 0, 0:SUB], ALU.pow).then_inc(rstd_ready, 1)

                rstd_of(0, 0)

                def batch(b, last):
                    for j in range(TILES):
                        t = b * TILES + j
                        if not (last and j == TILES - 1):
                            rstd_of(t + 1, j + 1)
                        pool.wait_ge(soft_ready, t + 1)
                        pool.tensor_tensor(active[:, :, :].rearrange("p s e -> p (s e)"), softplus[:, :, :].rearrange("p s e -> p (s e)"),
                                           powers[:, 1, :], ALU.pow).then_inc(active_ready, 1)

                batch(0, False)
                with pool.Fori(1, B - 1) as b:
                    batch(b, False)
                batch(B - 1, True)

            @block.scalar
            def _(act):
                def round_xt(t, j):
                    act.wait_ge(xt_ready, t + 1)
                    act.activation(xt_hi[:, j % 2].rearrange("p c t -> p (c t)"), ps_t.rearrange("p c t -> p (c t)"),
                                   ACT.Copy).then_inc(xt_hi_ready, 1)

                round_xt(0, 0)

                def round_qk(b, t, m):
                    act.wait_ge(qk_ready, t * 4 + m + 1)
                    wait(act, qk_out[m], t * 32)
                    act.activation(qk_hi[:, m, :], ps_a[:, m % 2, :], ACT.Identity, bias=a["bqk_sb"][:, m:m + 1]).then_inc(qk_hi_ready, 1)

                def batch(b, last):
                    for j in range(TILES):
                        t = b * TILES + j
                        act.preload_act_table_set(LN_SET)
                        round_qk(b, t, 0)
                        act.wait_ge(router_step, t * ROUTER_STEPS + 1)
                        act.activation(ex[:, :, :], absl[:, :, :], ACT.Exp, scale=-1.0).then_inc(exp_ready, 1)
                        round_qk(b, t, 1)
                        round_qk(b, t, 2)
                        act.wait_ge(router_step, t * ROUTER_STEPS + 2)
                        act.activation(logs[:, :, :], one_ex[:, :, :], ACT.Ln).then_inc(log_ready, 1)
                        round_qk(b, t, 3)
                        for e in range(NX):
                            act.wait_ge(hidden_ready, t * NX + e + 1)
                            if e == 0:
                                wait(act, unit_ready, t * SUB * UNITS)
                            act.activation(hid[:, e, :], ps_a[:, e % 2, :], ACT.Silu, bias=a["b1_sb"][:, e:e + 1]).then_inc(silu_done, 1)
                        if not (last and j == TILES - 1):
                            round_xt(t + 1, j + 1)

                batch(0, False)
                with act.Fori(1, B - 1) as b:
                    batch(b, False)
                batch(B - 1, True)

            @block.tensor
            def _(pe):
                w_hi, w_lo = a["w_hi"], a["w_lo"]

                def transpose_x(t, j):
                    pe.wait_ge(xn_ready, t + 1)
                    wait(pe, xt_lo_ready, t)
                    for s in range(SUB):
                        for c in range(EC):
                            last = pe.transpose(ps_t[:, c, s * P:(s + 1) * P], xn[:, j % 2, s, c * P:(c + 1) * P], a["ident_sb"][:, :])
                    last.then_inc(xt_ready, 1)

                transpose_x(0, 0)

                def exact(out, lhs, rhs):
                    terms = [(c, l, r) for c in range(EC) for l, r in ((0, 0), (1, 0), (0, 1))]
                    for k, (c, l, r) in enumerate(terms):
                        mm = pe.matmul(out, lhs[l](c), rhs[r](c), start=(k == 0), stop=(k == len(terms) - 1))
                    return mm

                def batch(b, last):
                    for j in range(TILES):
                        t = b * TILES + j
                        xt = [lambda c, lo=0, n=P, part=part, k=j % 2: part[:, k, c, lo:lo + n] for part in (xt_hi, xt_lo)]
                        pe.wait_ge(xt_hi_ready, t + 1)
                        pe.wait_ge(xt_lo_ready, t + 1)
                        for s in range(SUB):
                            if s < 2:
                                wait(pe, gate_t_out, t)
                            wait(pe, vr_out, t * SUB + s - 1 if s >= 2 else t * SUB)
                            exact(ps_v[:, s % 2, 0:VR],
                                  [lambda c, f=f, s=s: f(c, s * P, P) for f in xt],
                                  [lambda c, w=w: w[:, c, VR_COL:VR_COL + VR] for w in (w_hi, w_lo)]).then_inc(vr_ready, 1)
                        for m in range(4):
                            if m < 2:
                                wait(pe, silu_done, t * NX)
                            else:
                                pe.wait_ge(qk_lo_ready, t * 4 + m - 1)
                            exact(ps_a[:, m % 2, :],
                                  [lambda c, w=w, m=m: w[:, c, m * P:(m + 1) * P] for w in (w_hi, w_lo)],
                                  [lambda c, f=f: f(c, 0, TOK) for f in xt]).then_inc(qk_ready, 1)
                        for e in range(NX):
                            if e < 2:
                                pe.wait_ge(qk_lo_ready, t * 4 + 3 + e)
                            else:
                                pe.wait_ge(silu_done, t * NX + e - 1)
                            exact(ps_a[:, e % 2, :],
                                  [lambda c, w=w, e=e: w[:, c, W1_COL + e * FH:W1_COL + (e + 1) * FH] for w in (w_hi, w_lo)],
                                  [lambda c, f=f: f(c, 0, TOK) for f in xt]).then_inc(hidden_ready, 1)
                        if not (last and j == TILES - 1):
                            transpose_x(t + 1, j + 1)
                        pe.wait_ge(gate_ready, t + 1)
                        pe.wait_ge(vr_out, (t + 1) * SUB)
                        for s in range(SUB):
                            mm = pe.matmul(ps_v[0:NE + 2, 0, s * P:(s + 1) * P], gate[:, j % 2, s, :], a["ident_sb"][:, :], start=True, stop=True)
                        mm.then_inc(gate_t_ready, 1)
                        for s in range(SUB):
                            for u in range(UNITS):
                                n = s * UNITS + u
                                wait(pe, unit_out, t * SUB * UNITS + n - 1 if n else t * SUB * UNITS)
                                for k, e in enumerate(range(2 * u, min(2 * u + 2, NX))):
                                    pe.wait_ge(silu_done, t * NX + NX)
                                    out = ps_y[:, n % 2, k * E:(k + 1) * E]
                                    mm = pe.matmul(out, hid[:, e, s * P:(s + 1) * P], a["w2_sb"][:, e, :], start=True, stop=(e > 0))
                                    if e == 0:
                                        pe.wait_ge(gate_t_out, t + 1)
                                        mm = pe.matmul(out, gate_t[:, s * P:(s + 1) * P], a["b2_sb"][:, :], start=False, stop=True)
                                mm.then_inc(unit_ready, 1)

                batch(0, False)
                with pe.Fori(1, B - 1) as b:
                    batch(b, False)
                batch(B - 1, True)

            @block.vector
            def _(dve):
                def means(t, j, slot):
                    for s in range(SUB):
                        last = dve.bn_stats(stats[:, s, :], x[:, slot, s, :])
                    last.then_inc(stats_ready, 1)
                    dve.wait_ge(stats_ready, t + 1)
                    dve.memset(spare[:, :], 0.0)
                    for s in range(SUB):
                        last = dve.bn_aggr(mean_var[:, j % 2, s, :], stats[:, s, :])
                    last.then_inc(mean_ready, 1)

                def normalise(t, j, slot):
                    dve.wait_ge(rstd_ready, t + 1)
                    for s in range(SUB):
                        last = dve.tensor_scalar(xn[:, j % 2, s, :], x[:, slot, s, :], mean_var[:, j % 2, s, 0:1],
                                                 rstd[:, j % 2, s:s + 1], ALU.subtract, ALU.mult)
                    last.then_inc(xn_ready, 1)

                def low_xt(t, j):
                    dve.wait_ge(xt_hi_ready, t + 1)
                    dve.tensor_tensor(xt_lo[:, j % 2], ps_t, xt_hi[:, j % 2].bitcast(F32), ALU.subtract).then_inc(xt_lo_ready, 1)

                dve.wait_ge(const_ready, 1)
                dve.wait_ge(x_in[0], 16)
                means(0, 0, 0)
                normalise(0, 0, 0)
                low_xt(0, 0)

                def batch(b, last):
                    for j in range(TILES):
                        t = b * TILES + j
                        more = not (last and j == TILES - 1)
                        router = iter(range(1, ROUTER_STEPS + 1))

                        def step(ins):
                            ins.then_inc(router_step, 1)
                            dve.wait_ge(router_step, t * ROUTER_STEPS + next(router))

                        if more:
                            dve.wait_ge(x_in[(j + 1) % 4], (b + (j + 1) // 4) * 16 + 16)
                            means(t + 1, j + 1, (j + 1) % 4)
                        wait(dve, v_out[j], b * 16)
                        for s in range(SUB):
                            dve.wait_ge(vr_ready, t * SUB + s + 1)
                            if s == 0:
                                wait(dve, exp_ready, t)
                            dve.tensor_tensor(v[:, :, j * SUB + s, :], ps_v[:, s % 2, 0:E].rearrange("p (h d) -> p h d", h=H),
                                              a["bvr_sb"][:, 0:E].rearrange("p (h d) -> p h d", h=H), ALU.add)
                            dve.tensor_tensor(logit[:, s, :], ps_v[:, s % 2, E:VR], a["bvr_sb"][:, E:VR], ALU.add).then_inc(vr_out, 1)
                        dve.wait_ge(vr_out, (t + 1) * SUB)
                        step(dve.scalar_tensor_tensor(out=absl[:, :, :], in0=logit[:, :, :], scalar=-1.0, in1=logit[:, :, :],
                                                      op0=ALU.mult, op1=ALU.max))

                        def low_qk(m):
                            dve.wait_ge(qk_hi_ready, t * 4 + m + 1)
                            dve.scalar_tensor_tensor(out=qk_lo[:, m, :], in0=ps_a[:, m % 2, :], scalar=a["bqk_sb"][:, m:m + 1],
                                                     in1=qk_hi[:, m, :].bitcast(F32), op0=ALU.add,
                                                     op1=ALU.subtract).then_inc(qk_lo_ready, 1)

                        low_qk(0)
                        dve.wait_ge(exp_ready, t + 1)
                        step(dve.tensor_scalar(one_ex[:, :, :], ex[:, :, :], 1.0, None, ALU.add))
                        low_qk(1)
                        step(dve.scalar_tensor_tensor(out=lost[:, :, :], in0=one_ex[:, :, :], scalar=-1.0, in1=ex[:, :, :],
                                                      op0=ALU.add, op1=ALU.subtract))
                        dve.reciprocal(inv[:, :, :], one_ex[:, :, :])
                        low_qk(2)
                        step(dve.tensor_scalar(soft[:, :, :], logit[:, :, :], 0.0, None, ALU.max))
                        step(dve.tensor_tensor(lost[:, :, :], lost[:, :, :], inv[:, :, :], ALU.mult))
                        dve.wait_ge(log_ready, t + 1)
                        step(dve.tensor_tensor(log_soft[:, :, :], logs[:, :, :], lost[:, :, :], ALU.subtract))
                        dve.tensor_tensor(softplus[:, :, :], log_soft[:, :, :], soft[:, :, :], ALU.add).then_inc(soft_ready, 1)
                        low_qk(3)
                        if more:
                            normalise(t + 1, j + 1, (j + 1) % 4)
                        dve.wait_ge(active_ready, t + 1)
                        mine = active[:, :, :].rearrange("p s (e o) -> p s e o", o=1).broadcast_to([P, SUB, NE, NE])
                        other = active[:, :, :].rearrange("p s (o e) -> p s o e", o=1).broadcast_to([P, SUB, NE, NE])
                        dve.tensor_tensor(above[:, :, :, :], other, mine, ALU.is_gt)
                        step(dve.tensor_tensor(level[:, :, :, :], other, mine, ALU.is_equal))
                        earlier = a["earlier_sb"][:, :].rearrange("p (o e f) -> p o e f", o=1, e=NE).broadcast_to([P, SUB, NE, NE])
                        step(dve.tensor_tensor(level[:, :, :, :], level[:, :, :, :], earlier, ALU.mult))
                        step(dve.tensor_tensor(above[:, :, :, :], above[:, :, :, :], level[:, :, :, :], ALU.add))
                        dve.tensor_reduce(rank[:, :, :], above[:, :, :, :], AX.X, ALU.add).then_inc(rank_ready, 1)
                        dve.wait_ge(rank_ready, t + 1)
                        dve.scalar_tensor_tensor(out=gate[:, j % 2, :, 0:NE], in0=rank[:, :, :], scalar=2.0, in1=active[:, :, :],
                                                 op0=ALU.is_lt, op1=ALU.mult).then_inc(gate_ready, 1)
                        dve.wait_ge(gate_t_ready, t + 1)
                        dve.tensor_copy(gate_t[0:NE + 2, :], ps_v[0:NE + 2, 0, :]).then_inc(gate_t_out, 1)
                        if more:
                            low_xt(t + 1, j + 1)
                        if j < 2:
                            wait(dve, y_out[j % 2], b * 32)
                        else:
                            dve.wait_ge(y_out[j % 2], b * 32 + 16)
                        for s in range(SUB):
                            for u in range(UNITS):
                                n = s * UNITS + u
                                dve.wait_ge(unit_ready, t * SUB * UNITS + n + 1)
                                for k, e in enumerate(range(2 * u, min(2 * u + 2, NX))):
                                    out, part = y[:, j % 2, s, :], ps_y[:, n % 2, k * E:(k + 1) * E]
                                    if e == 0:
                                        ins = dve.tensor_tensor(out, part, x[:, j, s, :], ALU.add)
                                    else:
                                        if k == 1:
                                            dve.wait_ge(y_step, (t * SUB + s) * (UNITS - 1) + u + 1)
                                        else:
                                            dve.wait_ge(unit_out, (t * SUB + s) * UNITS + u)
                                        ins = dve.scalar_tensor_tensor(out=out, in0=part, scalar=gate[:, j % 2, s, e - 1:e],
                                                                       in1=out, op0=ALU.mult, op1=ALU.add)
                                    if k == 0 and e < NX - 1:
                                        ins.then_inc(y_step, 1)
                                ins.then_inc(unit_out, 1)

                batch(0, False)
                with dve.Fori(1, B - 1) as b:
                    batch(b, False)
                batch(B - 1, True)


def attention(nc, a, every_key):
    run = "again_" if every_key else ""
    with ExitStack() as ctx:
        sem = lambda name: ctx.enter_context(nc.semaphore(run + name))
        sb = lambda name, shape, dt=F32: ctx.enter_context(nc.sbuf_tensor("sb_" + run + name, shape, dt))
        Q, K = 0, 1
        GROUPS = 4 if every_key else 1
        rows_a = [[sb(f"{w}a{s}", [P, S], F32R) for s in range(2)] for w in "qk"]
        rows_b = [[sb(f"{w}b{s}", [P, S], F32R) for s in range(2)] for w in "qk"]
        src = [sb(f"{w}_src", [GROWS, S], F32R) for w in "qk"]
        hel_w = sb("hel_w", [GROWS, 2, P], F32R)
        comp = sb("comp", [P, 2, 2, HALF])
        sq_x = sb("sq_x", [P, 2, HALF])
        sq_y = sb("sq_y", [P, 2, HALF])
        norm2 = sb("norm2", [P, 2, HALF])
        log_n = sb("log_n", [P, HALF])
        rough = sb("rough", [P, 2, HALF])
        fine = sb("fine", [P, 2, HALF])
        inv_norm = sb("inv_norm", [P, 2, HALF])
        probs = sb("probs", [P, 2, S])
        v_raw = sb("v_raw", [P, 2, TB, D])
        v_ones = sb("v_ones", [P, 2, TB, 32])
        o_sb = sb("o_sb", [P, 2, 512])
        size = sb("size", [P, 512])
        abs_o = sb("abs_o", [P, 512])
        size_col = sb("size_col", [P, 1])
        ones_col = sb("ones_col", [P, 1])
        row_max = sb("row_max", [P, GROUPS, TB])
        best = sb("best", [P, TB])
        shift_hi = sb("shift_hi", [TB, P], F32R)
        shift_lo = sb("shift_lo", [TB, P], F32R)
        log_shift = sb("log_shift", [P, 1])
        three = sb("three", [P, 1])

        ps = ctx.enter_context(nc.psum_tensor(run + "ps_attention", [P, 8, 512], F32))
        ps_s, ps_o, ps_h = ps[:, 0:4, :], ps[:, 4:6, :], ps[:, 6:8, :]

        const_ready, hel_w_in = sem("att_const_ready"), sem("hel_w_in")
        src_in, rows_in = [sem("q_src_in"), sem("k_src_in")], [sem("rows_in0"), sem("rows_in1")]
        v_in, o_stored = [sem("v_in0"), sem("v_in1")], [sem("o_stored0"), sem("o_stored1")]
        scores_ready, exp_done, pv_done, hel_ready, hel_out = (
            sem("scores_ready"), sem("exp_done"), sem("pv_done"), sem("hel_ready"), sem("hel_out"))
        sq_x_ready, sq_y_ready, sum_ready, norm_ready, log_ready, rough_ready = (
            sem("sq_x_ready"), sem("sq_y_ready"), sem("sum_ready"), sem("norm_ready"), sem("log_n_ready"), sem("rough_ready"))
        v_ones_zero = sem("v_ones_zero")
        fine_step, inv_ready, unit_ready, round_ready, features_ready, o_ready, v_ones_ready = (
            sem("fine_step"), sem("inv_ready"), sem("unit_len_ready"), sem("round_ready"), sem("features_ready"),
            sem("o_ready"), sem("v_ones_ready"))
        max_ready, max_taken, best_ready, shift_ready, shift_hi_ready, shift_done = (
            sem("max_ready"), sem("max_taken"), sem("best_ready"), sem("shift_ready"), sem("shift_hi_ready"), sem("shift_done"))
        shift_in = [sem("shift_in0"), sem("shift_in1")]
        abs_ready = sem("abs_ready")
        size_ready, size_col_ready, total_ready, flag_ready = (
            sem("size_ready"), sem("size_col_ready"), sem("total_ready"), sem("flag_ready"))
        QUADS = TB // 4 * GROUPS * (4 if every_key else 1)
        ROWS_IN, SRC_IN = 4 * 16, 4 * 16

        with nc.Block() as block:

            @block.sync
            def _(sp):
                def load_src(n):
                    for which, scratch in ((Q, a["QS"]), (K, a["KS"])):
                        t, part = src[which], scratch[bass.ds(n, 1)]
                        both, hi = part.rearrange("o a d t -> (o a d) t"), part[:, 0].rearrange("o d t -> (o d) t")
                        for dst, rows in ((t[0:2 * D, :], both), (t[2 * D:3 * D, :], hi),
                                          (t[3 * D:5 * D, 0:S - 1], both[:, 1:S]), (t[5 * D:6 * D, 0:S - 1], hi[:, 1:S])):
                            sp.dma_start(dst.bitcast(F32), rows).then_inc(src_in[which], 16)
                    sp.dma_start(hel_w[:, :, :].bitcast(F32),
                                 a["WS"][bass.ds(n, 1)].rearrange("o k (c m) -> (o k) c m", c=2)).then_inc(hel_w_in, 16)

                def load_v(n, s):
                    sp.dma_start(v_raw[:, s], a["VS"][bass.ds(n, 1)].rearrange("o p (k d) -> (o p) k d", k=TB)).then_inc(v_in[s], 16)

                def load_rows(n, s):
                    q, k = a["QS"][bass.ds(n, 1)], a["KS"][bass.ds(n, 1)]
                    qb, kb = rows_b[Q][s], rows_b[K][s]
                    for dst, rows in ((qb[HX:HX + 2 * D, :], q.rearrange("o a d t -> (o a d) t")),
                                      (qb[HX + 2 * D:HX + 3 * D, :], q[:, 0].rearrange("o d t -> (o d) t")),
                                      (kb[HX:HX + D, :], k[:, 0].rearrange("o d t -> (o d) t")),
                                      (kb[HX + D:HX + 3 * D, :], k.rearrange("o a d t -> (o a d) t"))):
                        sp.dma_start(dst.bitcast(F32), rows).then_inc(rows_in[s], 16)

                def load_shift(n, s):
                    sp.wait_ge(shift_done, n + 1)
                    for r, part in enumerate((shift_hi, shift_lo)):
                        row = HX + 3 * D + r
                        sp.dma_start(rows_b[Q][s][row:row + 1, :].bitcast(F32).rearrange("o (k t) -> o k t", t=P), part[:, :].bitcast(F32)).then_inc(shift_in[s], 16)

                sp.wait_ge(const_ready, 1)
                load_src(0)
                load_v(0, 0)
                load_rows(0, 0)
                sp.wait_ge(hel_ready, 4)
                load_src(1)
                load_v(1, 1)
                load_shift(0, 0)

                def pair(i, last):
                    for s in range(2):
                        n = i * 2 + s
                        if not (last and s == 1):
                            wait(sp, scores_ready, n * 2 * TB)
                            load_rows(n + 1, 1 - s)
                        if not last:
                            sp.wait_ge(hel_ready, (n + 2) * 4)
                            load_src(n + 2)
                            sp.wait_ge(v_ones_ready, n + 1)
                            load_v(n + 2, s)
                        if not (last and s == 1):
                            load_shift(n + 1, 1 - s)
                        sp.wait_ge(o_ready, n + 1)
                        sp.dma_start(a["OS"][bass.ds(n, 1)].rearrange("o p t -> (o p) t"), o_sb[:, s, :]).then_inc(o_stored[s], 16)

                pair(0, False)
                with sp.Fori(1, NH // 2 - 1) as i:
                    pair(i, False)
                pair(NH // 2 - 1, True)
                for s in range(2):
                    sp.wait_ge(o_stored[s], NH // 2 * 16)

            @block.gpsimd
            def _(pool):
                def newton(h, which):
                    k = (2 * h + which) * 3
                    pool.wait_ge(rough_ready, 2 * h + which + 1)
                    pool.tensor_tensor(fine[:, which], rough[:, which], rough[:, which], ALU.mult).then_inc(fine_step, 1)
                    pool.wait_ge(fine_step, k + 1)
                    pool.tensor_tensor(fine[:, which], fine[:, which], norm2[:, which], ALU.mult).then_inc(fine_step, 1)
                    pool.wait_ge(fine_step, k + 2)
                    pool.tensor_tensor(fine[:, which], fine[:, which], three[:, :].broadcast_to([P, HALF]), ALU.subtract).then_inc(fine_step, 1)
                    pool.wait_ge(fine_step, k + 3)
                    pool.tensor_tensor(inv_norm[:, which], rough[:, which], fine[:, which], ALU.mult).then_inc(inv_ready, 1)

                pool.wait_ge(const_ready, 1)
                newton(0, Q)
                newton(0, K)

                def pair(i, last):
                    for s in range(2):
                        n = i * 2 + s
                        if not (last and s == 1):
                            newton(n + 1, Q)
                            newton(n + 1, K)

                pair(0, False)
                with pool.Fori(1, NH // 2 - 1) as i:
                    pair(i, False)
                pair(NH // 2 - 1, True)

            @block.scalar
            def _(act):
                act.preload_act_table_set(LN_SET)
                act.wait_ge(const_ready, 1)

                def exp(g, parity):
                    for half in range(2):
                        act.wait_ge(scores_ready, 2 * g + half + 1)
                        act.activation(probs[:, parity, half * HALF:(half + 1) * HALF],
                                       ps_s[:, 2 * half:2 * half + 2, :].rearrange("p c t -> p (c t)"), ACT.Exp,
                                       scale=0.125).then_inc(exp_done, 1)

                def square(h, which):
                    act.wait_ge(hel_out, 4 * h + 2 * which + 2)
                    act.activation(sq_y[:, which], comp[:, which, 1], ACT.Square).then_inc(sq_y_ready, 1)

                def log(h, which):
                    act.wait_ge(norm_ready, 2 * h + which + 1)
                    act.activation(log_n[:, :], norm2[:, which], ACT.Ln, scale=LOG_SCALE).then_inc(log_ready, 1)

                def power(h, which):
                    act.wait_ge(log_ready, 2 * h + which + 1)
                    act.activation(rough[:, which], log_n[:, :], ACT.Exp, bias=log_shift[:, 0:1], scale=-0.5).then_inc(rough_ready, 1)

                PREPARE = {2: (square, Q), 3: (log, Q), 4: (power, Q), 5: (square, K), 6: (log, K), 7: (power, K)}
                for slot in PREPARE:
                    PREPARE[slot][0](0, PREPARE[slot][1])
                exp(0, 0)

                def pair(i, last):
                    act.preload_act_table_set(LN_SET)
                    for s in range(2):
                        n = i * 2 + s
                        for tb in range(TB):
                            if last and s == 1 and tb == TB - 1:
                                break
                            exp(n * TB + tb + 1, (tb + 1) % 2)
                            if tb in PREPARE and not (last and s == 1):
                                PREPARE[tb][0](n + 1, PREPARE[tb][1])

                pair(0, False)
                with act.Fori(1, NH // 2 - 1) as i:
                    pair(i, False)
                pair(NH // 2 - 1, True)

            @block.tensor
            def _(pe):
                def score(g, s, tb, first=False):
                    for half in range(2):
                        if not first:
                            pe.wait_ge(exp_done, 2 * g - 1 + half)
                        for rows, start in ((rows_a, True), (rows_b, False)):
                            k = P if start else HX + 3 * D + 2
                            for c in (2 * half, 2 * half + 1):
                                mm = pe.matmul(ps_s[:, c, :], rows[K][s][0:k, tb * P:(tb + 1) * P],
                                               rows[Q][s][0:k, c * 512:(c + 1) * 512], start=start, stop=not start)
                        mm.then_inc(scores_ready, 1)

                def weigh(g, n, s, tb, parity):
                    if tb == 0:
                        pe.wait_ge(v_ones_ready, n + 1)
                        wait(pe, o_ready, n)
                    for c in range(4):
                        if c % 2 == 0:
                            pe.wait_ge(exp_done, 2 * g + c // 2 + 1)
                        mm = pe.matmul(ps_o[32 * c:32 * c + 32, s, :], v_ones[:, s, tb, :], probs[:, parity, c * 512:(c + 1) * 512],
                                       start=(tb == 0), stop=(tb == TB - 1), tile_position=(0, 32 * c))
                    mm.then_inc(pv_done, 1)

                def helical(h, which, chunk):
                    g = 4 * h + 2 * which + chunk
                    if chunk == 0:
                        pe.wait_ge(src_in[which], (h + 1) * SRC_IN)
                        if which == Q:
                            pe.wait_ge(hel_w_in, (h + 1) * 16)
                    wait(pe, hel_out, g)
                    if which == Q and chunk == 0:
                        wait(pe, shift_done, h)
                    for c in range(2):
                        mm = pe.matmul(ps_h[:, c, :], hel_w[:, c, :], src[which][:, chunk * 1024:(chunk + 1) * 1024:2],
                                       start=True, stop=True)
                    mm.then_inc(hel_ready, 1)

                def maxima(h, s, quad, uses):
                    if quad == 0:
                        pe.wait_ge(rows_in[s], uses * ROWS_IN)
                        pe.wait_ge(hel_out, 4 * (h + 1))
                    elif quad > 1:
                        pe.wait_ge(max_taken, QUADS * h + quad - 1)
                    q, k = rows_b[Q][s][HX:HX + 3 * D, :], rows_b[K][s][HX:HX + 3 * D, :]
                    if every_key:
                        blk, grp = quad // GROUPS, quad % GROUPS
                        mm = pe.matmul(ps_h[:, quad % 2, :], q[:, blk * P:(blk + 1) * P], k[:, grp * 512:(grp + 1) * 512],
                                       start=True, stop=True)
                    else:
                        for r in range(4):
                            blk = 4 * quad + r
                            mm = pe.matmul(ps_h[:, quad % 2, r * P:(r + 1) * P], q[:, blk * P:(blk + 1) * P], k[:, 0:S:TB],
                                           start=True, stop=True)
                    mm.then_inc(max_ready, 1)

                def turn_maxima(h):
                    pe.wait_ge(best_ready, h + 1)
                    pe.matmul(ps_h[0:TB, 0, 0:P], best[:, :], a["ident_sb"][:, :], start=True, stop=True).then_inc(shift_ready, 1)

                def all_maxima(h, s, uses, part, parts):
                    for quad in range(QUADS * part // parts, QUADS * (part + 1) // parts):
                        maxima(h, s, quad, uses)

                MAXIMA = (5, 6, 7, 8)
                HELICAL = {0: (Q, 0), 1: (Q, 1), 2: (K, 0), 3: (K, 1)}
                for which, chunk in HELICAL.values():
                    helical(0, which, chunk)
                all_maxima(0, 0, 1, 0, 1)
                turn_maxima(0)
                pe.wait_ge(features_ready, 2)
                pe.wait_ge(shift_in[0], 32)
                score(0, 0, 0, first=True)

                def pair(i, last):
                    for s in range(2):
                        n = i * 2 + s
                        more = not (last and s == 1)
                        for tb in range(TB):
                            g = n * TB + tb
                            if tb < TB - 1:
                                score(g + 1, s, tb + 1)
                            elif more:
                                pe.wait_ge(features_ready, 2 * (n + 2))
                                pe.wait_ge(shift_in[1 - s], (i + 1 + s) * 32)
                                score(g + 1, 1 - s, 0)
                            if tb in HELICAL and more:
                                helical(n + 1, *HELICAL[tb])
                            if tb in MAXIMA and more:
                                all_maxima(n + 1, 1 - s, i + 1 + s, tb - MAXIMA[0], len(MAXIMA))
                            if tb == MAXIMA[-1] + 1 and more:
                                turn_maxima(n + 1)
                            weigh(g, n, s, tb, tb % 2)

                pair(0, False)
                with pe.Fori(1, NH // 2 - 1) as i:
                    pair(i, False)
                pair(NH // 2 - 1, True)
                pe.wait_ge(size_col_ready, 1)
                pe.matmul(ps_h[0:1, 0, 0:1], size_col[:, :], ones_col[:, :], start=True, stop=True).then_inc(total_ready, 1)

            @block.vector
            def _(dve):
                for which in (Q, K):
                    dve.memset(src[which][6 * D:GROWS, :].bitcast(F32), 1.0)
                for s in range(2):
                    dve.memset(rows_b[K][s][96:P, :].bitcast(F32), 1.0)
                dve.memset(v_ones[:, :, :, :], 0.0).then_inc(v_ones_zero, 1)
                dve.wait_ge(v_ones_zero, 1)
                dve.memset(v_ones[:, :, :, D:D + 1], 1.0)
                dve.memset(three[:, :], 3.0)
                dve.memset(size[:, :], 0.0)
                dve.memset(ones_col[:, :], 1.0)
                dve.memset(log_shift[:, :], LOG_SHIFT).then_inc(const_ready, 1)

                def take(h, which, chunk):
                    dve.wait_ge(hel_ready, 4 * h + 2 * which + chunk + 1)
                    dve.tensor_copy(comp[:, which, :, chunk * 512:(chunk + 1) * 512], ps_h).then_inc(hel_out, 1)

                def square(h, which):
                    dve.wait_ge(hel_out, 4 * h + 2 * which + 2)
                    dve.tensor_tensor(sq_x[:, which], comp[:, which, 0], comp[:, which, 0], ALU.mult).then_inc(sq_x_ready, 1)

                def norm(h, which):
                    dve.wait_ge(sq_x_ready, 2 * h + which + 1)
                    dve.wait_ge(sq_y_ready, 2 * h + which + 1)
                    dve.tensor_tensor(sq_x[:, which], sq_x[:, which], sq_y[:, which], ALU.add).then_inc(sum_ready, 1)
                    dve.wait_ge(sum_ready, 2 * h + which + 1)
                    dve.tensor_scalar(norm2[:, which], sq_x[:, which], NORM_EPS2, None, ALU.max).then_inc(norm_ready, 1)

                def copy_v(h, s, loads):
                    dve.wait_ge(v_in[s], loads * 16)
                    dve.tensor_copy(v_ones[:, s, :, 0:D], v_raw[:, s]).then_inc(v_ones_ready, 1)

                def features(h, which, s):
                    n = 2 * h + which
                    unit = comp[:, which].rearrange("p c t -> p (c t)")
                    ra, rb = rows_a[which][s], rows_b[which][s]
                    dve.wait_ge(inv_ready, n + 1)
                    inv = inv_norm[:, which].rearrange("p (o t) -> p o t", o=1).broadcast_to([P, 2, HALF])
                    dve.scalar_tensor_tensor(out=comp[:, which], in0=comp[:, which], scalar=-0.0625 if which == Q else -0.5,
                                             in1=inv, op0=ALU.mult, op1=ALU.mult).then_inc(unit_ready, 1)
                    dve.wait_ge(unit_ready, n + 1)
                    dve.tensor_copy(ra[:, :], unit).then_inc(round_ready, 1)
                    dve.wait_ge(round_ready, n + 1)
                    if which == Q:
                        dve.tensor_tensor(ra[HX:P, :], unit[HX:P], ra[HX:P, :].bitcast(F32), ALU.subtract)
                        last = dve.tensor_copy(rb[0:HX, :], unit[0:HX])
                    else:
                        last = dve.tensor_tensor(rb[0:HX, :], unit[0:HX], ra[0:HX, :].bitcast(F32), ALU.subtract)
                    last.then_inc(features_ready, 1)

                def take_maxima(h):
                    for quad in range(QUADS):
                        dve.wait_ge(max_ready, QUADS * h + quad + 1)
                        if every_key:
                            out, scores = row_max[:, quad % GROUPS, quad // GROUPS:quad // GROUPS + 1], ps_h[:, quad % 2, :]
                        else:
                            out, scores = row_max[:, 0, 4 * quad:4 * quad + 4], ps_h[:, quad % 2, :].rearrange("p (r t) -> p r t", r=4)
                        dve.tensor_reduce(out, scores, AX.X, ALU.max).then_inc(max_taken, 1)
                    dve.wait_ge(max_taken, QUADS * (h + 1))
                    dve.tensor_reduce(best[:, :], row_max[:, :, :].rearrange("p g k -> p k g"), AX.X, ALU.max).then_inc(best_ready, 1)

                def split_maxima(h, s, uses):
                    dve.wait_ge(shift_ready, h + 1)
                    if uses is not None:
                        dve.wait_ge(shift_in[1 - s], uses * 32)
                    dve.tensor_scalar(shift_hi[:, :], ps_h[0:TB, 0, 0:P], -1.0, None, ALU.mult).then_inc(shift_hi_ready, 1)
                    dve.wait_ge(shift_hi_ready, h + 1)
                    dve.scalar_tensor_tensor(out=shift_lo[:, :], in0=ps_h[0:TB, 0, 0:P], scalar=-1.0, in1=shift_hi[:, :].bitcast(F32),
                                             op0=ALU.mult, op1=ALU.subtract).then_inc(shift_done, 1)

                def prepare(h, s, uses):
                    take(h, Q, 0)
                    take(h, Q, 1)
                    square(h, Q)
                    take(h, K, 0)
                    norm(h, Q)
                    take(h, K, 1)
                    square(h, K)
                    norm(h, K)
                    take_maxima(h)
                    features(h, Q, s)
                    split_maxima(h, s, uses)
                    features(h, K, s)

                dve.wait_ge(const_ready, 1)
                copy_v(0, 0, 1)
                prepare(0, 0, None)

                def pair(i, last):
                    for s in range(2):
                        n = i * 2 + s
                        if not (last and s == 1):
                            copy_v(n + 1, 1 - s, i + 1 + s)
                            prepare(n + 1, 1 - s, i + 1)
                        dve.wait_ge(pv_done, (n + 1) * TB)
                        wait(dve, o_stored[s], i * 16)
                        dve.tensor_copy(o_sb[:, s, :], ps_o[:, s, :]).then_inc(o_ready, 1)
                        dve.wait_ge(o_ready, n + 1)
                        wait(dve, size_ready, n)
                        dve.scalar_tensor_tensor(out=abs_o[:, :], in0=o_sb[:, s, :], scalar=-1.0, in1=o_sb[:, s, :], op0=ALU.mult,
                                                 op1=ALU.max).then_inc(abs_ready, 1)
                        dve.wait_ge(abs_ready, n + 1)
                        dve.tensor_tensor(size[:, :], size[:, :], abs_o[:, :], ALU.add).then_inc(size_ready, 1)

                pair(0, False)
                with dve.Fori(1, NH // 2 - 1) as i:
                    pair(i, False)
                pair(NH // 2 - 1, True)
                dve.wait_ge(size_ready, NH)
                dve.tensor_reduce(size_col[:, :], size[:, :], AX.X, ALU.add).then_inc(size_col_ready, 1)
                dve.wait_ge(total_ready, 1)
                dve.tensor_scalar(a["flag"][:, :], ps_h[0:1, 0, 0:1], SAFE, None, ALU.is_lt).then_inc(flag_ready, 1)
                dve.wait_ge(flag_ready, 1)


def project(nc, a):
    with ExitStack() as ctx:
        sem = lambda name: ctx.enter_context(nc.semaphore(name))
        sb = lambda name, shape, dt=F32: ctx.enter_context(nc.sbuf_tensor("sb_" + name, shape, dt))
        wo = sb("wo", [P, EC, E])
        sums = sb("sums", [P, 2, 512])
        inv = sb("inv_sums", [P, 2, 512])
        heads = sb("heads", [P, 3, EC, TOK])
        scale = sb("scale", [P, 3, EC, TOK])
        part = sb("part", [P, 3, SUB, E])
        normed = sb("normed", [P, 2, EC, TOK])
        out = sb("out_sb", [P, 2, SUB, E])
        ps = ctx.enter_context(nc.psum_tensor("ps_project", [P, 2, 2, 512], F32))
        wo_in, sums_in, inv_done, inv_out = sem("wo_in"), sem("sums_in"), sem("inv_done"), sem("inv_out")
        heads_in, scale_in, part_in = ([sem(f"{w}_in{j}") for j in range(3)] for w in ("heads", "scale", "part"))
        normed_ready, out_mm, out_ready = sem("normed_ready"), sem("out_mm"), sem("out_ready")
        out_stored = [sem("out_stored0"), sem("out_stored1")]
        T = B * TILES
        with nc.Block() as block:

            @block.sync
            def _(sp):
                sp.dma_start(wo[:, :, :], a["woT"].rearrange("(c p) n -> p c n", p=P)).then_inc(wo_in, 16)
                den = a["OS"].rearrange("n (c r) t -> n c r t", c=4)
                for k in range(2):
                    sp.dma_start(sums[:, k, :], den[k * 32:(k + 1) * 32, :, D, :]).then_inc(sums_in, 16)
                sp.wait_ge(inv_done, 1)
                for k in range(2):
                    sp.dma_start(a["RS"][k * 32:(k + 1) * 32], inv[:, k, :]).then_inc(inv_out, 16)
                sp.wait_ge(inv_out, 32)
                for t in range(T):
                    b, j, slot = t // TILES, t % TILES, t % 3
                    if t >= 3:
                        sp.wait_ge(normed_ready, t - 2)
                        sp.wait_ge(out_ready, (t - 2) * 2)
                    for c in range(EC):
                        h = b * H + c * 8
                        sp.dma_start(heads[:, slot, c, :], a["OS"][h:h + 8, 32 * j:32 * j + D, :]).then_inc(heads_in[slot], 16)
                        sp.dma_start(scale[:, slot, c, :],
                                     a["RS"][h:h + 8, j:j + 1, :].broadcast_to([8, D, 512])).then_inc(scale_in[slot], 16)
                    sp.dma_start(part[:, slot], a["PART"][t * TOK:(t + 1) * TOK, :].rearrange("(s p) e -> p s e", p=P)).then_inc(part_in[slot], 16)

            @block.scalar
            def _(act):
                for t in range(T):
                    act.wait_ge(out_ready, (t + 1) * 2)
                    act.dma_start(a["out"][t * TOK:(t + 1) * TOK, :].rearrange("(s p) e -> p s e", p=P), out[:, t % 2]).then_inc(out_stored[t % 2], 16)
                for j in range(2):
                    act.wait_ge(out_stored[j], T // 2 * 16)

            @block.tensor
            def _(pe):
                pe.wait_ge(wo_in, 16)
                for t in range(T):
                    pe.wait_ge(normed_ready, t + 1)
                    for s in range(SUB):
                        if s % 2 == 0 and t >= 2:
                            pe.wait_ge(out_ready, (t - 2) * 2 + s // 2 + 1)
                        for c in range(EC):
                            mm = pe.matmul(ps[:, t % 2, s // 2, (s % 2) * E:(s % 2 + 1) * E], normed[:, t % 2, c, s * P:(s + 1) * P],
                                           wo[:, c, :], start=(c == 0), stop=(c == EC - 1))
                        if s % 2:
                            mm.then_inc(out_mm, 1)

            @block.vector
            def _(dve):
                dve.wait_ge(sums_in, 32)
                dve.reciprocal(inv[:, :, :], sums[:, :, :]).then_inc(inv_done, 1)

                def scale_tile(t):
                    slot = t % 3
                    dve.wait_ge(heads_in[slot], (t // 3 + 1) * 32)
                    dve.wait_ge(scale_in[slot], (t // 3 + 1) * 32)
                    if t >= 2:
                        dve.wait_ge(out_mm, (t - 1) * 2)
                    dve.tensor_tensor(normed[:, t % 2], heads[:, slot], scale[:, slot], ALU.mult).then_inc(normed_ready, 1)

                scale_tile(0)
                for t in range(T):
                    if t + 1 < T:
                        scale_tile(t + 1)
                    dve.wait_ge(part_in[t % 3], (t // 3 + 1) * 16)
                    if t >= 2:
                        dve.wait_ge(out_stored[t % 2], t // 2 * 16)
                    for k in range(2):
                        dve.wait_ge(out_mm, t * 2 + k + 1)
                        dve.tensor_tensor(out[:, t % 2, 2 * k:2 * k + 2, :].rearrange("p s e -> p (s e)"), ps[:, t % 2, k, :],
                                          part[:, t % 3, 2 * k:2 * k + 2, :].rearrange("p s e -> p (s e)"), ALU.add).then_inc(out_ready, 1)


INPUTS = {
    "x": (N, E), "wcat": (E, WCOLS), "hel_w": (GROWS, H * 2 * P), "low_row": (GROWS, 1), "ident": (P, P),
    "w2": (FH, NX, E), "b2": (P, E), "bqk": (P, 4), "b1": (FH, NX), "bvr": (VR,), "earlier": (NE * NE,), "woT": (E, E),
}
SCRATCH = {
    "QS": (NH, 2, D, S), "KS": (NH, 2, D, S),
    "VS": (NH, P, TB * D), "WS": (NH, GROWS, 2 * P), "OS": (NH, P, 512), "RS": (NH, 4, 512),
    "PART": (N, E),
}


def build(nc):
    a = {name: nc.dram_tensor(name, shape, F32, kind="ExternalInput").ap() for name, shape in INPUTS.items()}
    a["out"] = nc.dram_tensor("out", (N, E), F32, kind="ExternalOutput").ap()
    for name, shape in SCRATCH.items():
        a[name] = nc.dram_tensor(name, shape, F32, kind="Internal").ap()
    a["ident_sb"] = nc.alloc_sbuf_tensor("sb_ident", [P, P], F32)
    a["flag"] = nc.alloc_sbuf_tensor("sb_flag", [1, 1], mybir.dt.int32)
    with ExitStack() as ctx:
        for name, shape, dt in (("w_hi", [P, EC, WCOLS], F32R), ("w_lo", [P, EC, WCOLS], F32R), ("w2_sb", [FH, NX, E], F32),
                                ("b2_sb", [P, E], F32), ("bqk_sb", [P, 4], F32),
                                ("b1_sb", [P, NX], F32), ("bvr_sb", [P, VR], F32), ("earlier_sb", [P, NE * NE], F32)):
            a[name] = ctx.enter_context(nc.sbuf_tensor("sb_" + name, shape, dt))
        split_weights(nc, a)
        tokens(nc, a)
    attention(nc, a, every_key=False)
    safe = nc.values_load(a["flag"][0:1, 0:1], min_val=0, max_val=1)
    with nc.If(safe == 0):
        attention(nc, a, every_key=True)
    project(nc, a)


def kernel(**inputs):
    import concourse.bacc as bacc
    from concourse.bass_utils import run_bass_kernel_spmd

    w = {k: np.asarray(v) for k, v in inputs.items()}
    g = lambda name: w["L0_" + name]
    f = np.float32
    hel_w = np.zeros((GROWS, H, 2, 2, 2, HX // 2), f)
    whel = g("attn_Whel").reshape(H, HX // 2, 2, D).transpose(3, 0, 2, 1)[:, :, :, None, :]
    bhel = g("attn_bhel").reshape(H, HX // 2, 2).transpose(0, 2, 1)
    for parity in range(2):
        for k in range(3):
            r = (3 * parity + k) * D
            hel_w[r:r + D, :, :, :, parity, :] = whel
    hel_w[6 * D:, :] = bhel[None, :, :, None, None, :]
    low_row = np.zeros((GROWS, 1), f)
    for r in (2 * D, 5 * D):
        low_row[r:r + D] = -1.0
    low_row[6 * D + 1] = -1.0
    b2 = np.zeros((P, E), f)
    b2[:NE], b2[NE], b2[NE + 1] = g("ffn_rb2"), g("ffn_sb2"), g("attn_bo")
    arrays = {
        "x": g("attn_x").reshape(N, E),
        "wcat": np.concatenate([g("attn_Wq").T, g("attn_Wk").T, g("attn_Wv").T, g("ffn_routing_W").T, g("ffn_sW1"),
                                g("ffn_rW1").transpose(1, 0, 2).reshape(E, NE * FH)], axis=1),
        "hel_w": hel_w.reshape(GROWS, -1), "low_row": low_row, "ident": np.eye(P, dtype=f),
        "w2": np.concatenate([g("ffn_sW2")[None], g("ffn_rW2")]).transpose(1, 0, 2), "b2": b2,
        "bqk": np.concatenate([g("attn_bq"), g("attn_bk")]).reshape(4, P).T,
        "b1": np.concatenate([g("ffn_sb1")[None], g("ffn_rb1")]).T,
        "bvr": np.concatenate([g("attn_bv"), g("ffn_expert_bias")]),
        "earlier": np.tril(np.ones((NE, NE), f), -1).reshape(-1),
        "woT": g("attn_Wo").T,
    }
    arrays = {k: np.ascontiguousarray(v) for k, v in arrays.items()}
    nc = bacc.Bacc("TRN2", target_bir_lowering=False, num_devices=1)
    build(nc)
    r = run_bass_kernel_spmd(nc, [arrays], core_ids=[0])
    return r.results[0]["out"].reshape(B, S, E)
```
